# Optimizing a Trainium2 kernel written in Bass

```python
import numpy as np
import jax
import jax.numpy as jnp

def _softmax(x, axis=-1):
    return jax.nn.softmax(x, axis=axis)

def _gelu(x):
    return jax.nn.gelu(x, approximate=True)

def _silu(x):
    return jax.nn.silu(x)

def _sigmoid(x):
    return jax.nn.sigmoid(x)

def _layernorm(x, axis=-1, eps=1e-05):
    m = jnp.mean(x, axis=axis, keepdims=True)
    v = jnp.var(x, axis=axis, keepdims=True)
    return (x - m) / jnp.sqrt(v + eps)

def _scatter_add(tgt, idx, src, axis=0):
    return tgt.at[idx].add(src)

def _segment_sum(src, seg, n):
    return jax.ops.segment_sum(src, seg, n)
kernel_name = 'mk_vit_tower_cls_d1_tok_img1024_r4_7347ae'

def setup_inputs(seed: int=0):
    np.random.seed(seed)
    _w = jnp.asarray

    def _rec_inputs():
        import jax
        import jax.numpy as jnp
        _rk = jax.random.key(seed)
        x = -0.00016672 + 0.999947 * jax.random.normal(jax.random.fold_in(_rk, 1), (16, 3, 112, 112), jnp.float32)
        cls_tok = 0.02 * jax.random.normal(jax.random.fold_in(_rk, 5), (1, 1, 256), jnp.float32)
        return (x, cls_tok)
    x, cls_tok = _rec_inputs()

    def _L0_tok_setup():
        import jax, jax.numpy as jnp
        import numpy as np
        IMG = 96
        PATCH = 16
        CIN = 3
        DIM = 256
        B = 64
        key = jax.random.key(seed)
        k1, k2 = jax.random.split(key)
        x = jax.random.normal(k1, (B, CIN, IMG, IMG), dtype=jnp.float32)
        W = jax.random.normal(k2, (DIM, PATCH * PATCH * CIN), dtype=jnp.float32) * 0.02
        return {'x': x, 'W': W}
    _L0_tok_all = _L0_tok_setup()
    _L0_tok_in = {k: v for k, v in _L0_tok_all.items() if k in ('W',)}
    del _L0_tok_all

    def _L0_attn_setup():
        import jax, jax.numpy as jnp
        import numpy as np
        D_MODEL = 256
        N_HEADS = 16
        HEAD_DIM = D_MODEL // N_HEADS
        ROPE_BASE = 10000.0

        def rotate_half(x):
            d = x.shape[-1]
            x1, x2 = (x[..., :d // 2], x[..., d // 2:])
            return jnp.concatenate((-x2, x1), axis=-1)

        def rope_cos_sin(T, dim, dtype):
            inv_freq = 1.0 / ROPE_BASE ** (jnp.arange(0, dim, 2, dtype=jnp.float32) / dim)
            t = jnp.arange(T, dtype=jnp.float32)
            freqs = jnp.einsum('i,j->ij', t, inv_freq)
            emb = jnp.concatenate((freqs, freqs), axis=-1)
            return (jnp.cos(emb).astype(dtype), jnp.sin(emb).astype(dtype))
        key = jax.random.key(seed)
        ks = jax.random.split(key, 9)
        s = 0.02
        return {'x': jax.random.normal(ks[0], (4, 512, D_MODEL), dtype=jnp.float32), 'Wq': jax.random.normal(ks[1], (D_MODEL, D_MODEL), dtype=jnp.float32) * s, 'bq': jax.random.normal(ks[2], (D_MODEL,), dtype=jnp.float32) * s, 'Wk': jax.random.normal(ks[3], (D_MODEL, D_MODEL), dtype=jnp.float32) * s, 'bk': jax.random.normal(ks[4], (D_MODEL,), dtype=jnp.float32) * s, 'Wv': jax.random.normal(ks[5], (D_MODEL, D_MODEL), dtype=jnp.float32) * s, 'bv': jax.random.normal(ks[6], (D_MODEL,), dtype=jnp.float32) * s, 'Wo': jax.random.normal(ks[7], (D_MODEL, D_MODEL), dtype=jnp.float32) * s, 'bo': jax.random.normal(ks[8], (D_MODEL,), dtype=jnp.float32) * s}
    _L0_attn_all = _L0_attn_setup()
    _L0_attn_in = {k: v for k, v in _L0_attn_all.items() if k in ('Wq', 'bq', 'Wk', 'bk', 'Wv', 'bv', 'Wo', 'bo')}
    del _L0_attn_all

    def _L0_ffn_setup():
        import jax, jax.numpy as jnp
        import numpy as np
        H = 256
        M = 128
        E = 16
        TOP_K = 2
        SCALE = 2.5
        NORM_TOPK = True
        B, S = (1, 256)

        def _moe(x, gate_w, w_gate, w_up, w_down, ws_gate, ws_up, ws_down):
            T = x.shape[0]
            shared = jax.nn.silu(x @ ws_gate) * (x @ ws_up) @ ws_down
            scores = jax.nn.sigmoid(x.astype(jnp.float32) @ gate_w.T.astype(jnp.float32))
            topk_w, topk_idx = jax.lax.top_k(scores, TOP_K)
            if NORM_TOPK and TOP_K > 1:
                topk_w = topk_w / (topk_w.sum(-1, keepdims=True) + 1e-20)
            topk_w = topk_w * SCALE
            route = jnp.zeros((T, E), topk_w.dtype).at[jnp.arange(T)[:, None], topk_idx].set(topk_w)
            g = jnp.einsum('th,ehm->etm', x, w_gate)
            u = jnp.einsum('th,ehm->etm', x, w_up)
            eo = jnp.einsum('etm,emh->eth', jax.nn.silu(g) * u, w_down)
            routed = jnp.einsum('te,eth->th', route.astype(x.dtype), eo)
            return routed + shared
        key = jax.random.key(seed)
        ks = jax.random.split(key, 8)
        std = 0.02
        return {'hidden_states': jax.random.normal(ks[0], (B, S, H), jnp.float32), 'gate_w': jax.random.normal(ks[1], (E, H), jnp.float32) * std, 'w_gate': jax.random.normal(ks[2], (E, H, M), jnp.float32) * std, 'w_up': jax.random.normal(ks[3], (E, H, M), jnp.float32) * std, 'w_down': jax.random.normal(ks[4], (E, M, H), jnp.float32) * std, 'ws_gate': jax.random.normal(ks[5], (H, M), jnp.float32) * std, 'ws_up': jax.random.normal(ks[6], (H, M), jnp.float32) * std, 'ws_down': jax.random.normal(ks[7], (M, H), jnp.float32) * std}
    _L0_ffn_all = _L0_ffn_setup()
    _L0_ffn_in = {k: v for k, v in _L0_ffn_all.items() if k in ('gate_w', 'w_gate', 'w_up', 'w_down', 'ws_gate', 'ws_up', 'ws_down')}
    del _L0_ffn_all
    return {'x': x, 'cls_tok': cls_tok, 'L0_tok_W': _L0_tok_in['W'], 'L0_attn_Wq': _L0_attn_in['Wq'], 'L0_attn_bq': _L0_attn_in['bq'], 'L0_attn_Wk': _L0_attn_in['Wk'], 'L0_attn_bk': _L0_attn_in['bk'], 'L0_attn_Wv': _L0_attn_in['Wv'], 'L0_attn_bv': _L0_attn_in['bv'], 'L0_attn_Wo': _L0_attn_in['Wo'], 'L0_attn_bo': _L0_attn_in['bo'], 'L0_ffn_gate_w': _L0_ffn_in['gate_w'], 'L0_ffn_w_gate': _L0_ffn_in['w_gate'], 'L0_ffn_w_up': _L0_ffn_in['w_up'], 'L0_ffn_w_down': _L0_ffn_in['w_down'], 'L0_ffn_ws_gate': _L0_ffn_in['ws_gate'], 'L0_ffn_ws_up': _L0_ffn_in['ws_up'], 'L0_ffn_ws_down': _L0_ffn_in['ws_down']}

def reference(x, cls_tok, L0_tok_W, L0_attn_Wq, L0_attn_bq, L0_attn_Wk, L0_attn_bk, L0_attn_Wv, L0_attn_bv, L0_attn_Wo, L0_attn_bo, L0_ffn_gate_w, L0_ffn_w_gate, L0_ffn_w_up, L0_ffn_w_down, L0_ffn_ws_gate, L0_ffn_ws_up, L0_ffn_ws_down):
    import jax
    import jax.numpy as jnp

    def _L0_tok_ref(x, W):
        import jax, jax.numpy as jnp
        import numpy as np
        IMG = 96
        PATCH = 16
        CIN = 3
        DIM = 256
        B = 64
        B_, C, H, Wd = x.shape
        p = PATCH
        nh, nw = (H // p, Wd // p)
        patches = x.reshape(B_, C, nh, p, nw, p)
        patches = patches.transpose(0, 2, 4, 1, 3, 5)
        patches = patches.reshape(B_, nh * nw, C * p * p)
        return jnp.einsum('bnd,kd->bnk', patches, W)

    def _L0_attn_ref(x, Wq, bq, Wk, bk, Wv, bv, Wo, bo):
        import jax, jax.numpy as jnp
        import numpy as np
        D_MODEL = 256
        N_HEADS = 16
        HEAD_DIM = D_MODEL // N_HEADS
        ROPE_BASE = 10000.0

        def rotate_half(x):
            d = x.shape[-1]
            x1, x2 = (x[..., :d // 2], x[..., d // 2:])
            return jnp.concatenate((-x2, x1), axis=-1)

        def rope_cos_sin(T, dim, dtype):
            inv_freq = 1.0 / ROPE_BASE ** (jnp.arange(0, dim, 2, dtype=jnp.float32) / dim)
            t = jnp.arange(T, dtype=jnp.float32)
            freqs = jnp.einsum('i,j->ij', t, inv_freq)
            emb = jnp.concatenate((freqs, freqs), axis=-1)
            return (jnp.cos(emb).astype(dtype), jnp.sin(emb).astype(dtype))
        B, T, D = x.shape
        H, hd = (N_HEADS, HEAD_DIM)

        def proj(W, b):
            y = jnp.einsum('btd,ed->bte', x, W) + b
            return y.reshape(B, T, H, hd).transpose(0, 2, 1, 3)
        q = proj(Wq, bq)
        k = proj(Wk, bk)
        v = proj(Wv, bv)
        cos, sin = rope_cos_sin(T, hd, x.dtype)
        q = q * cos + rotate_half(q) * sin
        k = k * cos + rotate_half(k) * sin
        scores = jnp.einsum('bhqd,bhkd->bhqk', q, k) / jnp.sqrt(jnp.asarray(hd, x.dtype))
        causal = jnp.tril(jnp.ones((T, T), dtype=bool))
        scores = jnp.where(causal, scores, jnp.asarray(-jnp.inf, x.dtype))
        attn = jax.nn.softmax(scores, axis=-1)
        out = jnp.einsum('bhqk,bhkd->bhqd', attn, v)
        out = out.transpose(0, 2, 1, 3).reshape(B, T, D)
        return jnp.einsum('btd,ed->bte', out, Wo) + bo

    def _L0_ffn_ref(hidden_states, gate_w, w_gate, w_up, w_down, ws_gate, ws_up, ws_down):
        import jax, jax.numpy as jnp
        import numpy as np
        H = 256
        M = 128
        E = 16
        TOP_K = 2
        SCALE = 2.5
        NORM_TOPK = True
        B, S = (1, 256)

        def _moe(x, gate_w, w_gate, w_up, w_down, ws_gate, ws_up, ws_down):
            T = x.shape[0]
            shared = jax.nn.silu(x @ ws_gate) * (x @ ws_up) @ ws_down
            scores = jax.nn.sigmoid(x.astype(jnp.float32) @ gate_w.T.astype(jnp.float32))
            topk_w, topk_idx = jax.lax.top_k(scores, TOP_K)
            if NORM_TOPK and TOP_K > 1:
                topk_w = topk_w / (topk_w.sum(-1, keepdims=True) + 1e-20)
            topk_w = topk_w * SCALE
            route = jnp.zeros((T, E), topk_w.dtype).at[jnp.arange(T)[:, None], topk_idx].set(topk_w)
            g = jnp.einsum('th,ehm->etm', x, w_gate)
            u = jnp.einsum('th,ehm->etm', x, w_up)
            eo = jnp.einsum('etm,emh->eth', jax.nn.silu(g) * u, w_down)
            routed = jnp.einsum('te,eth->th', route.astype(x.dtype), eo)
            return routed + shared
        b, s, h = hidden_states.shape
        x = hidden_states.reshape(-1, h)
        out = _moe(x, gate_w, w_gate, w_up, w_down, ws_gate, ws_up, ws_down)
        return out.reshape(b, s, h)
    h = _L0_tok_ref(x, L0_tok_W)
    h = jnp.concatenate([jnp.broadcast_to(cls_tok, (h.shape[0], 1, h.shape[2])), h], axis=1)
    h = h + _L0_attn_ref(_layernorm(h, axis=-1), L0_attn_Wq, L0_attn_bq, L0_attn_Wk, L0_attn_bk, L0_attn_Wv, L0_attn_bv, L0_attn_Wo, L0_attn_bo)
    h = h + _L0_ffn_ref(_layernorm(h, axis=-1), L0_ffn_gate_w, L0_ffn_w_gate, L0_ffn_w_up, L0_ffn_w_down, L0_ffn_ws_gate, L0_ffn_ws_up, L0_ffn_ws_down)
    return h

_drawn_inputs = setup_inputs


def setup_inputs(seed=0):
    import zlib

    import numpy as np

    out = dict(_drawn_inputs(seed))
    spreads = {}
    factors = {'L0_attn_Wq': 8.0,
     'L0_attn_bq': 21.602,
     'L0_attn_Wk': 8.0,
     'L0_attn_bk': 35.423,
     'L0_attn_bv': 4.601,
     'L0_ffn_ws_gate': 2.67}
    for name, (base, spread) in spreads.items():
        noise = np.random.default_rng([zlib.crc32(name.encode()), seed]).standard_normal(out[name].shape)
        drawn = base * np.exp(spread * noise) if base else spread * noise
        out[name] = jnp.asarray(drawn.astype(out[name].dtype))
    for name, factor in factors.items():
        out[name] = (out[name] * factor).astype(out[name].dtype)
    return out
```

```python
from contextlib import ExitStack

import concourse.bass as bass
from concourse import mybir

F32 = mybir.dt.float32
BF16 = mybir.dt.bfloat16
ALU = mybir.AluOpType
ACT = mybir.ActivationFunctionType
AX = mybir.AxisListType

P = 128
BATCH = 16
SEQ = 50
DIM = 256
KD = DIM // P
HEADS = 16
HD = DIM // HEADS
TILES = BATCH // 2
TT = 2 * SEQ
SECOND = 64
ROWS = SECOND + SEQ
TOKENS = BATCH * SEQ
PATCH_IN = 768
KP = PATCH_IN // P
EXPERTS = 16
NEXP = EXPERTS + 1
FF = 128
WEXP = KD * 2 * FF + DIM
PAIRS = HEADS // 2
GROUPS = P // (2 * HD)
VCOL = 2 * HD + 2
HALF_TILES = TILES // 2
HALF = HALF_TILES * TT
EPS = 1e-5
LN_COUNT = DIM
SWAP = [(i // HD) * HD + (i + HD // 2) % HD for i in range(32)]


def vit_block(nc, x_patches, w_patch, cls_rows, w_q, w_k, w_v, w_o, biases, bo_row,
              w_experts, w_route, c_rope, c_ident, c_mask, c_spread, c_kmask, c_vmask, c_ones,
              c_iota, c_power, out):
    with ExitStack() as ctx:
        def sb(name, shape, dt=F32):
            return ctx.enter_context(nc.sbuf_tensor(name, shape, dt))

        def sem(name):
            return ctx.enter_context(nc.semaphore(name))

        bank = [ctx.enter_context(nc.psum_tensor(f"bank{i}", [P, 512], F32)) for i in range(4)]
        score_ps = ctx.enter_context(nc.psum_tensor("score_ps", [P, GROUPS, 512], F32))

        xp = sb("xp", [P, TILES, KP * TT])
        wp = sb("wp", [P, KP, DIM])
        cls = sb("cls", [TT, DIM])
        wq = sb("wq", [P, KD, DIM])
        wk = sb("wk", [P, KD, DIM])
        wv = sb("wv", [P, KD, DIM])
        wo = sb("wo", [P, KD, DIM])
        bias = sb("bias", [P, 6])
        bo = sb("bo", [TT, DIM])
        wexp = sb("wexp", [P, NEXP * WEXP])
        wroute = sb("wroute", [P, KD, EXPERTS])
        rope = sb("rope", [P, 2, SEQ])
        ident = sb("ident", [P, P])
        mask_f = sb("mask_f", [SEQ, 4 * SEQ])
        spread_f = sb("spread_f", [SEQ, ROWS])
        mask = sb("mask", [SEQ, 4 * SEQ], BF16)
        spread = sb("spread", [SEQ, ROWS], BF16)
        kmask = sb("kmask", [P, 2])
        vmask = sb("vmask", [TT, DIM])
        iota = sb("iota", [TT, EXPERTS])
        power = sb("power", [TT, 1])

        h = sb("h", [TT, TILES, DIM])
        hb = sb("hb", [TT, TILES, DIM])
        stats = sb("stats", [TT, 6])
        mv = sb("mv", [TT, 2 * TILES, 2])
        ve = sb("ve", [TT, 2 * TILES])
        rstd = sb("rstd", [TT, 2 * TILES])
        hln = sb("hln", [TT, 2, DIM])
        hlnT = sb("hlnT", [P, KD, TILES, TT])
        hlnD = sb("hlnD", [P, KD, BATCH, 2, SEQ])
        qb = sb("qb", [P, 2, HALF])
        qc = sb("qc", [P, 2, HALF])
        qs = sb("qs", [P, 2, HALF])
        qr = sb("qr", [P, 2, HALF])
        kf = sb("kf", [P, 2, HALF])
        qT = sb("qT", [P, KD, TILES, TT])
        kM = sb("kM", [P, KD, 2, TILES, TT])
        vbd = sb("vbd", [TT, BATCH, PAIRS, VCOL])
        spare = xp[0:ROWS, :, :].rearrange("p t d -> p (t d)")
        shifted = spare[:, 0:2 * HEADS * SEQ].rearrange("p (n s) -> p n s", n=2)
        probs = spare[:, 2 * HEADS * SEQ:4 * HEADS * SEQ].rearrange("p (n s) -> p n s", n=2)
        probsT = sb("probsT", [TT, 2, PAIRS, ROWS])
        mx = sb("mx", [ROWS, HEADS])
        rinv = sb("rinv", [ROWS, HEADS])
        attn = sb("attn", [ROWS, 2, DIM])
        attnT = sb("attnT", [P, KD, TILES, TT])
        sg = sb("sg", [TT, 2, FF])
        act_rows = sb("act_rows", [TT, 2, FF])
        actT = sb("actT", [P, 2, TT])
        ge = sb("ge", [TT, TILES, EXPERTS])
        gs = sb("gs", [TT, TILES, EXPERTS])
        one1 = sb("one1", [TT, TILES, EXPERTS])
        one2 = sb("one2", [TT, TILES, EXPERTS])
        rtmp = sb("rtmp", [TT, TILES, EXPERTS])
        top = sb("top", [TT, 8, TILES])
        route = sb("route", [TT, TILES, NEXP])

        x_in = [sem(f"x_in{t}") for t in range(TILES)]
        wp_in = sem("wp_in")
        small_in = sem("small_in")
        cls_in = sem("cls_in")
        ident_in = sem("ident_in")
        wqk_in = sem("wqk_in")
        wvo_in = sem("wvo_in")
        ones_in = sem("ones_in")
        wexp_in = sem("wexp_in")
        tok_done = sem("tok_done")
        h_ready = sem("h_ready")
        hb_ready = sem("hb_ready")
        dve_step = sem("dve_step")
        ve_ready = sem("ve_ready")
        rstd_ready = sem("rstd_ready")
        hln_ready = sem("hln_ready")
        lnT_done = sem("lnT_done")
        hlnT_ready = sem("hlnT_ready")
        hlnD_ready = sem("hlnD_ready")
        proj_done = sem("proj_done")
        qb_ready = sem("qb_ready")
        qc_ready = sem("qc_ready")
        rope_done = sem("rope_done")
        kM_ready = sem("kM_ready")
        v_done = sem("v_done")
        v_ready = sem("v_ready")
        mask_ready = sem("mask_ready")
        s_done = sem("s_done")
        shift_done = sem("shift_done")
        exp_done = sem("exp_done")
        pt_done = sem("pt_done")
        ptev_act = sem("ptev_act")
        ptev_dve = sem("ptev_dve")
        o_done = sem("o_done")
        o_ready = sem("o_ready")
        ot_done = sem("ot_done")
        attnT_ready = sem("attnT_ready")
        wo_done = sem("wo_done")
        h2_ready = sem("h2_ready")
        gate_done = sem("gate_done")
        gexp_ready = sem("gexp_ready")
        route_ready = sem("route_ready")
        gu_done = sem("gu_done")
        silu_ready = sem("silu_ready")
        act_ready = sem("act_ready")
        actT_done = sem("actT_done")
        actT_ready = sem("actT_ready")
        y_done = sem("y_done")
        acc_ready = sem("acc_ready")
        out_done = sem("out_done")

        block = ctx.enter_context(nc.Block())

        lnT_ps = [bank[2], bank[3]]

        def tile_scores():
            return score_ps[0:ROWS, :, 0:4 * SEQ].rearrange("p g (s k) -> p g s k", k=SEQ)

        @block.sync
        def _(sp):
            sp.dma_start(wp[:, :, :], w_patch).then_inc(wp_in, 16)
            for t in range(TILES):
                sp.dma_start(xp[:, t, :], x_patches[:, t, :]).then_inc(x_in[t], 16)
                if t == 0:
                    sp.dma_start(cls[:, :], cls_rows).then_inc(cls_in, 16)
                    sp.dma_start(power[:, :], c_power).then_inc(cls_in, 16)
                    sp.dma_start(ident[:, :], c_ident).then_inc(ident_in, 16)
            sp.dma_start(wq[:, :, :], w_q).then_inc(wqk_in, 16)
            sp.dma_start(wk[:, :, :], w_k).then_inc(wqk_in, 16)
            sp.dma_start(bias[:, :], biases).then_inc(small_in, 16)
            sp.dma_start(bo[:, :], bo_row.partition_broadcast(TT)).then_inc(small_in, 16)
            sp.dma_start(wroute[:, :, :], w_route).then_inc(small_in, 16)
            sp.dma_start(rope[:, :, :], c_rope).then_inc(small_in, 16)
            sp.dma_start(mask_f[:, :], c_mask).then_inc(small_in, 16)
            sp.dma_start(spread_f[:, :], c_spread).then_inc(small_in, 16)
            sp.dma_start(kmask[:, :], c_kmask).then_inc(small_in, 16)
            sp.dma_start(vmask[:, :], c_vmask).then_inc(small_in, 16)
            sp.dma_start(iota[:, :], c_iota).then_inc(small_in, 16)
            sp.dma_start(wv[:, :, :], w_v).then_inc(wvo_in, 16)
            sp.dma_start(wo[:, :, :], w_o).then_inc(wvo_in, 16)
            sp.dma_start(vbd[:, :, :, 2 * HD:VCOL],
                         c_ones.rearrange("p (b n j) -> p b n j", b=BATCH, n=PAIRS)).then_inc(ones_in, 16)
            sp.dma_start(wexp[:, :], w_experts).then_inc(wexp_in, 16)
            for t in range(TILES):
                sp.wait_ge(acc_ready, (NEXP - 1) * TILES + t + 1)
                sp.dma_start(out[t * TT:(t + 1) * TT, :], h[:, t, :]).then_inc(out_done, 16)
            sp.wait_ge(out_done, 16 * TILES)

        @block.gpsimd
        def _(pool):
            pool.wait_ge(cls_in, 32)
            for n in range(TILES):
                pool.wait_ge(ve_ready, n + 1)
                nc.gpsimd.tensor_tensor(rstd[:, n:n + 1], ve[:, n:n + 1], power[:, :], ALU.pow).then_inc(rstd_ready, 1)
            pool.wait_ge(small_in, 16 * 9)
            pool.wait_ge(h_ready, TILES)
            for t in range(TILES):
                nc.gpsimd.tensor_tensor(hb[:, t, :], h[:, t, :], bo[:, :], ALU.add).then_inc(hb_ready, 1)
            for j in range(8):
                pool.wait_ge(qb_ready, j + 1)
                cos = rope[:, 0:1, :].to_broadcast([P, HALF // SEQ, SEQ])
                nc.gpsimd.tensor_tensor(qc[:, j % 2, :].rearrange("p (b s) -> p b s", s=SEQ),
                                        qb[:, j % 2, :].rearrange("p (b s) -> p b s", s=SEQ),
                                        cos, ALU.mult).then_inc(qc_ready, 1)
            for n in range(TILES, 2 * TILES):
                pool.wait_ge(ve_ready, n + 1)
                nc.gpsimd.tensor_tensor(rstd[:, n:n + 1], ve[:, n:n + 1], power[:, :], ALU.pow).then_inc(rstd_ready, 1)

        @block.scalar
        def _(act):
            for t in range(TILES):
                act.wait_ge(lnT_done, t + 1)
                for c in range(KD):
                    src = lnT_ps[t % 2][:, c * TT:(c + 1) * TT].rearrange("p (b o s) -> p b o s", b=2, o=1)
                    nc.scalar.copy(hlnD[:, c, 2 * t:2 * t + 2, :, :],
                                   src.to_broadcast([P, 2, 2, SEQ])).then_inc(hlnD_ready, 1)
            act.wait_ge(small_in, 16 * 9)

            def mask_keys(j):
                half, c = j // 4, (j % 4) // 2
                act.wait_ge(rope_done, j + 1)
                for i in range(2):
                    dst = kM[:, c, i, half * HALF_TILES:(half + 1) * HALF_TILES, :].rearrange("p t s -> p (t s)")
                    nc.scalar.activation(dst, kf[:, (j // 2) % 2, :], ACT.Copy,
                                         scale=kmask[:, i:i + 1]).then_inc(kM_ready, 1)

            for j in range(8):
                act.wait_ge(proj_done, j + 1)
                if j >= 2:
                    act.wait_ge(rope_done, j - 1)
                nc.scalar.activation(qb[:, j % 2, :], bank[j % 2][:, 0:HALF], ACT.Identity,
                                     bias=bias[:, (j % 4):(j % 4) + 1]).then_inc(qb_ready, 1)
                if j >= 1 and (j - 1) % 2 == 1:
                    mask_keys(j - 1)
            mask_keys(7)

            def exponentials(t):
                act.wait_ge(shift_done, t + 1)
                if t >= 2:
                    act.wait_ge(pt_done, 2 * (t - 1))
                nc.scalar.activation(probs[:, t % 2, :], shifted[:, t % 2, :], ACT.Exp).then_inc(exp_done, 1)

            exponentials(0)
            for t in range(TILES):
                if t + 1 < TILES:
                    exponentials(t + 1)
                act.wait_ge(pt_done, 2 * t + 1)
                if t >= 2:
                    act.wait_ge(o_done, t - 1)
                nc.scalar.copy(probsT[:, t % 2, 0:GROUPS, :],
                               bank[0][0:TT, 0:GROUPS * ROWS].rearrange("p (n q) -> p n q", n=GROUPS)).then_inc(ptev_act, 1)
                act.wait_ge(ot_done, t + 1)
                for c in range(KD):
                    src = bank[3][:, c * ROWS:c * ROWS + ROWS]
                    for b in range(2):
                        nc.scalar.activation(attnT[:, c, t, b * SEQ:(b + 1) * SEQ],
                                             src[:, b * SECOND:b * SECOND + SEQ], ACT.Identity,
                                             bias=bias[:, 4 + c:5 + c]).then_inc(attnT_ready, 1)
            for t in range(TILES):
                act.wait_ge(lnT_done, TILES + t + 1)
                nc.scalar.copy(hlnT[:, :, t, :],
                               lnT_ps[t % 2][:, 0:KD * TT].rearrange("p (c s) -> p c s", c=KD)).then_inc(hlnT_ready, 1)
            act.wait_ge(gate_done, TILES)
            nc.scalar.activation(ge[:, :, :].rearrange("p t e -> p (t e)"), score_ps[0:TT, 0, 0:TILES * EXPERTS],
                                 ACT.Exp, scale=-1.0).then_inc(gexp_ready, 1)

            with act.Fori(0, NEXP) as e:
                for t in range(TILES + 1):
                    if t < TILES:
                        act.wait_ge(gu_done, e * TILES + (t + 1))
                        if t >= 2:
                            act.wait_ge(act_ready, e * TILES + (t - 1))
                        nc.scalar.activation(sg[:, t % 2, :], bank[t % 2][0:TT, 0:FF], ACT.Silu).then_inc(silu_ready, 1)
                    if t >= 1:
                        u = t - 1
                        act.wait_ge(actT_done, e * TILES + (u + 1))
                        if u >= 2:
                            act.wait_ge(y_done, e * TILES + (u - 1))
                        nc.scalar.copy(actT[:, u % 2, :], bank[2 + u % 2][:, 0:TT]).then_inc(actT_ready, 1)

        @block.vector
        def _(dve):
            steps = [0]

            def in_order(instruction):
                steps[0] += 1
                instruction.then_inc(dve_step, 1)
                dve.wait_ge(dve_step, steps[0])

            def statistics(n, rows):
                in_order(nc.vector.bn_stats(stats[:, :], rows))
                in_order(nc.vector.bn_aggr(mv[:, n, :], stats[:, :]))
                nc.vector.tensor_scalar_add(ve[:, n:n + 1], mv[:, n, 1:2], EPS).then_inc(ve_ready, 1)

            def normalise(n, t):
                dve.wait_ge(rstd_ready, n + 1)
                if n >= 2:
                    dve.wait_ge(lnT_done, n - 1)
                nc.vector.tensor_scalar(hln[:, t % 2, :], h[:, t, :], mv[:, n, 0:1], rstd[:, n:n + 1],
                                        ALU.subtract, ALU.mult).then_inc(hln_ready, 1)

            dve.wait_ge(cls_in, 32)
            for t in range(TILES + 1):
                if t < TILES:
                    dve.wait_ge(tok_done, t + 1)
                    nc.vector.tensor_tensor(h[:, t, :], bank[t % 2][0:TT, 0:DIM], cls[:, :], ALU.add).then_inc(h_ready, 1)
                    dve.wait_ge(h_ready, t + 1)
                    statistics(t, h[:, t, :])
                if t >= 1:
                    normalise(t - 1, t - 1)
            dve.wait_ge(small_in, 16 * 9)
            nc.vector.tensor_copy(mask[:, :], mask_f[:, :]).then_inc(mask_ready, 1)
            nc.vector.tensor_copy(spread[:, :], spread_f[:, :]).then_inc(mask_ready, 1)
            for j in range(8):
                half, c, keys = j // 4, (j % 4) // 2, j % 2
                dve.wait_ge(qb_ready, j + 1)
                in_order(nc.vector.stream_shuffle(qs[:, j % 2, :], qb[:, j % 2, :], SWAP))
                sine = rope[:, 1:2, :].to_broadcast([P, HALF // SEQ, SEQ])
                in_order(nc.vector.tensor_tensor(qr[:, j % 2, :].rearrange("p (b s) -> p b s", s=SEQ),
                                                 qs[:, j % 2, :].rearrange("p (b s) -> p b s", s=SEQ),
                                                 sine, ALU.mult))
                dve.wait_ge(qc_ready, j + 1)
                if keys:
                    if j >= 4:
                        dve.wait_ge(kM_ready, 2 * (j // 2 - 1))
                    dst = kf[:, (j // 2) % 2, :]
                else:
                    dst = qT[:, c, half * HALF_TILES:(half + 1) * HALF_TILES, :].rearrange("p t s -> p (t s)")
                nc.vector.tensor_tensor(dst, qc[:, j % 2, :], qr[:, j % 2, :], ALU.add).then_inc(rope_done, 1)
            for b in range(BATCH):
                dve.wait_ge(v_done, b + 1)
                nc.vector.tensor_tensor(vbd[:, b, :, 0:2 * HD],
                                        bank[2 + b % 2][0:TT, 0:DIM].rearrange("p (n d) -> p n d", n=PAIRS),
                                        vmask[:, :].rearrange("p (n d) -> p n d", n=PAIRS), ALU.mult).then_inc(v_ready, 1)

            def shift(t):
                dve.wait_ge(s_done, t + 1)
                in_order(nc.vector.tensor_reduce(mx[:, :].rearrange("p (g s) -> p g s", g=GROUPS), tile_scores(),
                                                 AX.X, ALU.max))
                if t >= 2:
                    dve.wait_ge(exp_done, t - 1)
                nc.vector.tensor_tensor(
                    shifted[:, t % 2, :].rearrange("p (g s k) -> p g s k", g=GROUPS, k=SEQ), tile_scores(),
                    mx[:, :].rearrange("p (g s o) -> p g s o", g=GROUPS, o=1).to_broadcast([ROWS, GROUPS, 4, SEQ]),
                    ALU.subtract).then_inc(shift_done, 1)

            shift(0)
            for t in range(TILES):
                if t + 1 < TILES:
                    shift(t + 1)
                dve.wait_ge(pt_done, 2 * t + 2)
                if t >= 2:
                    dve.wait_ge(o_done, t - 1)
                nc.vector.tensor_copy(probsT[:, t % 2, GROUPS:PAIRS, :],
                                      bank[1][0:TT, 0:GROUPS * ROWS].rearrange("p (n q) -> p n q", n=GROUPS)).then_inc(ptev_dve, 1)
                dve.wait_ge(o_done, t + 1)
                outs = bank[2][0:ROWS, 0:PAIRS * VCOL].rearrange("p (n v) -> p n v", v=VCOL)
                in_order(nc.vector.reciprocal(rinv[:, :].rearrange("p (n i) -> p n i", i=2), outs[:, :, 2 * HD:VCOL]))
                if t >= 2:
                    dve.wait_ge(ot_done, t - 1)
                nc.vector.tensor_tensor(
                    attn[:, t % 2, :].rearrange("p (n i d) -> p n i d", i=2, d=HD),
                    outs[:, :, 0:2 * HD].rearrange("p n (i d) -> p n i d", i=2),
                    rinv[:, :].rearrange("p (n i o) -> p n i o", i=2, o=1).to_broadcast([ROWS, PAIRS, 2, HD]),
                    ALU.mult).then_inc(o_ready, 1)

            dve.wait_ge(hb_ready, TILES)
            for t in range(TILES + 1):
                if t < TILES:
                    dve.wait_ge(wo_done, t + 1)
                    nc.vector.tensor_tensor(h[:, t, :], bank[t % 2][0:TT, 0:DIM], hb[:, t, :], ALU.add).then_inc(h2_ready, 1)
                    dve.wait_ge(h2_ready, t + 1)
                    statistics(TILES + t, h[:, t, :])
                if t >= 1:
                    normalise(TILES + t - 1, t - 1)

            dve.wait_ge(gexp_ready, 1)
            in_order(nc.vector.tensor_scalar_add(ge[:, :, :], ge[:, :, :], 1.0))
            in_order(nc.vector.reciprocal(gs[:, :, :], ge[:, :, :]))
            wide = [TT, TILES, EXPERTS]

            def column(i):
                return top[:, i, :].rearrange("p (t o) -> p t o", o=1).to_broadcast(wide)

            iotas = iota[:, :].rearrange("p (o e) -> p o e", o=1).to_broadcast(wide)

            def choose(i, onehot):
                in_order(nc.vector.tensor_reduce(top[:, i, :], gs[:, :, :], AX.X, ALU.max))
                in_order(nc.vector.tensor_tensor(rtmp[:, :, :], gs[:, :, :], column(i), ALU.is_equal))
                in_order(nc.vector.tensor_tensor(rtmp[:, :, :], rtmp[:, :, :], iotas, ALU.mult))
                in_order(nc.vector.tensor_reduce(top[:, i + 2, :], rtmp[:, :, :], AX.X, ALU.min))
                in_order(nc.vector.tensor_tensor(onehot[:, :, :], iotas, column(i + 2), ALU.is_equal))

            choose(0, one1)
            in_order(nc.vector.scalar_tensor_tensor(gs[:, :, :], one1[:, :, :], -4.0, gs[:, :, :], ALU.mult, ALU.add))
            choose(1, one2)
            in_order(nc.vector.tensor_tensor(top[:, 4, :], top[:, 0, :], top[:, 1, :], ALU.add))
            in_order(nc.vector.tensor_scalar_add(top[:, 4, :], top[:, 4, :], 1e-20))
            in_order(nc.vector.reciprocal(top[:, 5, :], top[:, 4, :]))
            for i in range(2):
                in_order(nc.vector.tensor_tensor(top[:, 6 + i, :], top[:, i, :], top[:, 5, :], ALU.mult))
                in_order(nc.vector.tensor_scalar_mul(top[:, 6 + i, :], top[:, 6 + i, :], 2.5))
            in_order(nc.vector.tensor_tensor(one1[:, :, :], one1[:, :, :], column(6), ALU.mult))
            in_order(nc.vector.tensor_tensor(one2[:, :, :], one2[:, :, :], column(7), ALU.mult))
            nc.vector.memset(route[:, :, EXPERTS:NEXP], 1.0).then_inc(route_ready, 1)
            nc.vector.tensor_tensor(route[:, :, 0:EXPERTS], one1[:, :, :], one2[:, :, :], ALU.add).then_inc(route_ready, 1)
            dve.wait_ge(route_ready, 2)

            with dve.Fori(0, NEXP) as e:
                for t in range(TILES + 2):
                    if t < TILES:
                        dve.wait_ge(silu_ready, e * TILES + (t + 1))
                        if t >= 2:
                            dve.wait_ge(actT_done, e * TILES + (t - 1))
                        nc.vector.tensor_tensor(act_rows[:, t % 2, :], sg[:, t % 2, :], bank[t % 2][0:TT, FF:2 * FF],
                                                ALU.mult).then_inc(act_ready, 1)
                    if t >= 2:
                        u = t - 2
                        dve.wait_ge(y_done, e * TILES + (u + 1))
                        weight = route[:, u, bass.ds(e, 1)]
                        nc.vector.scalar_tensor_tensor(h[:, u, :], score_ps[0:TT, u % 2, 0:DIM], weight, h[:, u, :],
                                                       ALU.mult, ALU.add).then_inc(acc_ready, 1)

        @block.tensor
        def _(pe):
            def transposes(n):
                t = n % TILES
                pe.wait_ge(hln_ready, n + 1)
                if n >= TILES + 2:
                    pe.wait_ge(hlnT_ready, n - TILES - 1)
                elif 2 <= n < TILES:
                    pe.wait_ge(hlnD_ready, KD * (n - 1))
                for c in range(KD):
                    last = nc.tensor.transpose(lnT_ps[t % 2][:, c * TT:(c + 1) * TT], hln[:, t % 2, c * P:(c + 1) * P],
                                               ident[0:TT, 0:TT])
                last.then_inc(lnT_done, 1)

            pe.wait_ge(wp_in, 16)
            pe.wait_ge(ident_in, 16)
            for t in range(TILES + 2):
                if t < TILES:
                    pe.wait_ge(x_in[t], 16)
                    if t >= 2:
                        pe.wait_ge(h_ready, t - 1)
                    for k in range(KP):
                        last = nc.tensor.matmul(bank[t % 2][0:TT, 0:DIM], xp[:, t, k * TT:(k + 1) * TT], wp[:, k, :],
                                                start=(k == 0), stop=(k == KP - 1))
                    last.then_inc(tok_done, 1)
                if t >= 2:
                    transposes(t - 2)

            pe.wait_ge(wqk_in, 32)
            pe.wait_ge(h_ready, TILES)
            pe.wait_ge(hlnD_ready, KD * TILES)
            for j in range(8):
                half, c, w = j // 4, (j % 4) // 2, (wq, wk)[j % 2]
                if j >= 2:
                    pe.wait_ge(qb_ready, j - 1)
                for k in range(KD):
                    last = nc.tensor.matmul(bank[j % 2][:, 0:HALF], w[:, k, c * P:(c + 1) * P],
                                            hlnD[:, k, 2 * half * HALF_TILES:2 * (half + 1) * HALF_TILES, 0, :],
                                            start=(k == 0), stop=(k == KD - 1))
                last.then_inc(proj_done, 1)

            pe.wait_ge(wvo_in, 32)
            for b in range(BATCH):
                if b >= 2:
                    pe.wait_ge(v_ready, b - 1)
                for k in range(KD):
                    last = nc.tensor.matmul(bank[2 + b % 2][0:TT, 0:DIM], hlnD[:, k, b, :, :], wv[:, k, :],
                                            start=(k == 0), stop=(k == KD - 1))
                last.then_inc(v_done, 1)

            pe.wait_ge(mask_ready, 2)
            pe.wait_ge(rope_done, 8)
            pe.wait_ge(kM_ready, 8)

            def scores(t):
                if t >= 1:
                    pe.wait_ge(shift_done, t)
                for g in range(GROUPS):
                    nc.tensor.matmul(score_ps[0:ROWS, g, 0:4 * SEQ], spread[:, :], mask[:, :],
                                     start=True, stop=False, skip_group_check=True)
                for c in range(KD):
                    for b in range(2):
                        for g in range(GROUPS):
                            rows = slice(2 * HD * g, 2 * HD * (g + 1))
                            last = nc.tensor.matmul(
                                score_ps[b * SECOND:b * SECOND + SEQ, g, c * 2 * SEQ:(c + 1) * 2 * SEQ],
                                qT[rows, c, t, b * SEQ:(b + 1) * SEQ], kM[rows, c, :, t, b * SEQ:(b + 1) * SEQ],
                                start=False, stop=True, skip_group_check=True)
                last.then_inc(s_done, 1)

            scores(0)
            pe.wait_ge(v_ready, BATCH)
            pe.wait_ge(ones_in, 16)
            for t in range(TILES):
                if t + 1 < TILES:
                    scores(t + 1)
                pe.wait_ge(exp_done, t + 1)
                for c in range(KD):
                    if t >= 1:
                        pe.wait_ge((ptev_act, ptev_dve)[c], t)
                    for g in range(GROUPS):
                        col = (g * KD + c) * 2 * SEQ
                        last = nc.tensor.transpose(bank[c][0:TT, g * ROWS:(g + 1) * ROWS],
                                                   probs[:, t % 2, col:col + 2 * SEQ], ident[0:ROWS, 0:ROWS])
                    last.then_inc(pt_done, 1)
                pe.wait_ge(ptev_act, t + 1)
                pe.wait_ge(ptev_dve, t + 1)
                if t >= 1:
                    pe.wait_ge(o_ready, t)
                for b in range(2):
                    width = SECOND if b == 0 else SEQ
                    for n in range(PAIRS):
                        last = nc.tensor.matmul(bank[2][b * SECOND:b * SECOND + width, n * VCOL:(n + 1) * VCOL],
                                                probsT[:, t % 2, n, b * SECOND:b * SECOND + width],
                                                vbd[:, 2 * t + b, n, :], start=True, stop=True)
                last.then_inc(o_done, 1)
                pe.wait_ge(o_ready, t + 1)
                if t >= 1:
                    pe.wait_ge(attnT_ready, 4 * t)
                for c in range(KD):
                    last = nc.tensor.transpose(bank[3][:, c * ROWS:(c + 1) * ROWS], attn[:, t % 2, c * P:(c + 1) * P],
                                               ident[0:ROWS, 0:ROWS])
                last.then_inc(ot_done, 1)

            def gate(t):
                pe.wait_ge(hlnT_ready, t + 1)
                for k in range(KD):
                    last = nc.tensor.matmul(score_ps[0:TT, 0, t * EXPERTS:(t + 1) * EXPERTS], hlnT[:, k, t, :],
                                            wroute[:, k, :], start=(k == 0), stop=(k == KD - 1))
                last.then_inc(gate_done, 1)

            pe.wait_ge(attnT_ready, 4 * TILES)
            for t in range(TILES + 3):
                if t < TILES:
                    if t >= 2:
                        pe.wait_ge(h2_ready, t - 1)
                    for k in range(KD):
                        last = nc.tensor.matmul(bank[t % 2][0:TT, 0:DIM], attnT[:, k, t, :], wo[:, k, :],
                                                start=(k == 0), stop=(k == KD - 1))
                    last.then_inc(wo_done, 1)
                if 2 <= t < TILES + 2:
                    transposes(TILES + t - 2)
                if t >= 3:
                    gate(t - 3)

            pe.wait_ge(wexp_in, 16)
            pe.wait_ge(gexp_ready, 1)
            pe.wait_ge(h2_ready, TILES)
            with pe.Fori(0, NEXP) as e:
                for t in range(TILES + 2):
                    if t < TILES:
                        if t >= 2:
                            pe.wait_ge(act_ready, e * TILES + (t - 1))
                        for k in range(KD):
                            last = nc.tensor.matmul(bank[t % 2][0:TT, 0:2 * FF], hlnT[:, k, t, :],
                                                    wexp[:, bass.ds(e * WEXP + k * 2 * FF, 2 * FF)],
                                                    start=(k == 0), stop=(k == KD - 1))
                        last.then_inc(gu_done, 1)
                    if 1 <= t < TILES + 1:
                        u = t - 1
                        pe.wait_ge(act_ready, e * TILES + (u + 1))
                        if u >= 2:
                            pe.wait_ge(actT_ready, e * TILES + (u - 1))
                        nc.tensor.transpose(bank[2 + u % 2][:, 0:TT], act_rows[:, u % 2, :],
                                            ident[0:TT, 0:TT]).then_inc(actT_done, 1)
                    if t >= 2:
                        u = t - 2
                        pe.wait_ge(actT_ready, e * TILES + (u + 1))
                        if u >= 2:
                            pe.wait_ge(acc_ready, e * TILES + (u - 1))
                        nc.tensor.matmul(score_ps[0:TT, u % 2, 0:DIM], actT[:, u % 2, :],
                                         wexp[:, bass.ds(e * WEXP + KD * 2 * FF, DIM)],
                                         start=True, stop=True).then_inc(y_done, 1)
                pe.wait_ge(acc_ready, e * TILES + TILES)


def laid_out(inputs):
    import numpy as np

    def f(name):
        return np.asarray(inputs[name])

    x = f("x")
    side = x.shape[2] // 16
    patches = x.reshape(BATCH, 3, side, 16, side, 16).transpose(0, 2, 4, 1, 3, 5).reshape(BATCH, SEQ - 1, PATCH_IN)
    rows = np.zeros((BATCH, SEQ, PATCH_IN), np.float32)
    rows[:, 1:] = patches
    x_patches = rows.reshape(TILES, TT, KP, P).transpose(3, 0, 2, 1).reshape(P, TILES, KP * TT)
    w_patch = f("L0_tok_W").T.reshape(KP, P, DIM).transpose(1, 0, 2)
    cls_rows = np.zeros((TT, DIM), np.float32)
    cls_rows[[0, SEQ]] = f("cls_tok").reshape(DIM)

    def projection(name):
        return f(name).T.reshape(KD, P, DIM).transpose(1, 0, 2)

    bq, bk, bv = (f(f"L0_attn_b{n}").reshape(KD, P) for n in "qkv")
    biases = np.stack([bq[0], bk[0], bq[1], bk[1], bv[0], bv[1]], axis=1)
    gate = np.concatenate([f("L0_ffn_w_gate"), f("L0_ffn_ws_gate")[None]]).reshape(NEXP, KD, P, FF)
    up = np.concatenate([f("L0_ffn_w_up"), f("L0_ffn_ws_up")[None]]).reshape(NEXP, KD, P, FF)
    down = np.concatenate([f("L0_ffn_w_down"), f("L0_ffn_ws_down")[None]])
    both = np.concatenate([gate, up], axis=3).transpose(2, 0, 1, 3).reshape(P, NEXP, KD * 2 * FF)
    w_experts = np.concatenate([both, down.transpose(1, 0, 2)], axis=2).reshape(P, NEXP * WEXP)
    w_route = f("L0_ffn_gate_w").T.reshape(KD, P, EXPERTS).transpose(1, 0, 2)

    inv = (np.float32(1.0) / np.power(np.float32(10000.0), np.arange(0, HD, 2, dtype=np.float32) / np.float32(HD))).astype(np.float32)
    angle = np.outer(np.arange(SEQ, dtype=np.float32), inv).astype(np.float32)
    angle = np.concatenate([angle, angle], axis=1)
    sign = np.where(np.arange(HD) < HD // 2, -1.0, 1.0).astype(np.float32)
    c_rope = np.stack([np.tile(np.cos(angle).T, (P // HD, 1)), np.tile((np.sin(angle) * sign).T, (P // HD, 1))], axis=1)
    later = np.arange(SEQ)[None, :] > np.arange(SEQ)[:, None]
    c_mask = np.tile(np.where(later, -1e30, 0.0), (1, 4))
    c_spread = np.zeros((SEQ, ROWS))
    c_spread[np.arange(SEQ), np.arange(SEQ)] = 1.0
    c_spread[np.arange(SEQ), SECOND + np.arange(SEQ)] = 1.0
    of_head = (np.arange(P) // HD) % 2
    c_kmask = np.stack([of_head == 0, of_head == 1], axis=1) * HD ** -0.5
    second_half = np.arange(TT) >= SEQ
    c_vmask = (second_half[:, None] == ((np.arange(DIM) // HD) % 2 == 1)[None, :]) * 1.0
    c_ones = np.tile(np.stack([~second_half, second_half], axis=1) * 1.0, (1, BATCH * PAIRS))
    c_iota = np.tile(np.arange(EXPERTS) - EXPERTS, (TT, 1))
    c_power = np.full((TT, 1), -0.5)
    arrays = dict(
        x_patches=x_patches, w_patch=w_patch, cls_rows=cls_rows,
        w_q=projection("L0_attn_Wq"), w_k=projection("L0_attn_Wk"), w_v=projection("L0_attn_Wv"),
        w_o=projection("L0_attn_Wo"), biases=biases, bo_row=f("L0_attn_bo"), w_experts=w_experts, w_route=w_route)
    tables = dict(
        c_rope=c_rope, c_ident=np.eye(P), c_mask=c_mask, c_spread=c_spread, c_kmask=c_kmask, c_vmask=c_vmask,
        c_ones=c_ones, c_iota=c_iota, c_power=c_power)
    arrays.update({n: a.astype(np.float32) for n, a in tables.items()})
    return {n: np.ascontiguousarray(a) for n, a in arrays.items()}


def kernel(**inputs):
    import concourse.bacc as bacc
    from concourse.bass_utils import run_bass_kernel_spmd

    nc = bacc.Bacc("TRN2", target_bir_lowering=False, num_devices=1)
    arrays = laid_out(inputs)
    args = [nc.dram_tensor(n, a.shape, F32, kind="ExternalInput").ap() for n, a in arrays.items()]
    out = nc.dram_tensor("out", (TOKENS, DIM), F32, kind="ExternalOutput").ap()
    vit_block(nc, *args, out)
    result = run_bass_kernel_spmd(nc, [arrays], core_ids=[0])
    return result.results[0]["out"].reshape(BATCH, SEQ, DIM)
```
